# Optimizing a Trainium2 kernel written in Bass

```python
import numpy as np
import jax
import jax.numpy as jnp

def _softmax(x, axis=-1):
    return jax.nn.softmax(x, axis=axis)

def _gelu(x):
    return jax.nn.gelu(x, approximate=True)

def _silu(x):
    return jax.nn.silu(x)

def _sigmoid(x):
    return jax.nn.sigmoid(x)

def _layernorm(x, axis=-1, eps=1e-05):
    m = jnp.mean(x, axis=axis, keepdims=True)
    v = jnp.var(x, axis=axis, keepdims=True)
    return (x - m) / jnp.sqrt(v + eps)

def _scatter_add(tgt, idx, src, axis=0):
    return tgt.at[idx].add(src)

def _segment_sum(src, seg, n):
    return jax.ops.segment_sum(src, seg, n)
kernel_name = 'mk_adj_resnorm_d1_adj_r2_5c7c2e'

def setup_inputs(seed: int=0):
    np.random.seed(seed)
    _w = jnp.asarray

    def _rec_inputs():
        import jax
        import jax.numpy as jnp
        _gk = jax.random.key(seed)
        x = 7.22e-05 + 1 * jax.random.normal(jax.random.fold_in(_gk, 1), (1354, 512), jnp.float32)
        _a = jax.random.bernoulli(jax.random.fold_in(_gk, 2), 0.0014771, (1354, 1354))
        _a = jnp.logical_or(_a, jnp.swapaxes(_a, -1, -2))
        _a = jnp.logical_or(_a, jnp.eye(1354, dtype=bool))
        _af = _a.astype(jnp.float32)
        _d = jnp.maximum(_af.sum(-1), 1.0) ** (-0.5)
        _af = _af * _d[..., :, None] * _d[..., None, :]
        adj = _af
        return (x, adj)
    x, adj = _rec_inputs()

    def _L0_gnn_setup():
        import jax, jax.numpy as jnp
        import numpy as np
        N = 4096
        D = 512

        def adjacent_mat(adj):
            adj = adj + jnp.eye(adj.shape[0], dtype=adj.dtype)
            deg = jnp.sum(adj, axis=1)
            dinv = jnp.where(deg > 0, deg ** (-0.5), 0.0).astype(adj.dtype)
            return dinv[:, None] * adj * dinv[None, :]
        key = jax.random.key(seed)
        k1, k2 = jax.random.split(key)
        x = jax.random.normal(k1, (N, D), dtype=jnp.float32)
        Coefficient2 = 1e-08 * jnp.ones((N, N), dtype=jnp.float32)
        A = jax.random.uniform(k2, (N, N), dtype=jnp.float32)
        return {'x': x, 'Coefficient2': Coefficient2, 'A': A}
    _L0_gnn_all = _L0_gnn_setup()
    _L0_gnn_in = {k: v for k, v in _L0_gnn_all.items() if k in ()}
    del _L0_gnn_all
    return {'x': x, 'adj': adj}

def reference(x, adj):
    import jax
    import jax.numpy as jnp

    def _L0_gnn_ref(x, Coefficient2, A):
        import jax, jax.numpy as jnp
        import numpy as np
        N = 4096
        D = 512

        def adjacent_mat(adj):
            adj = adj + jnp.eye(adj.shape[0], dtype=adj.dtype)
            deg = jnp.sum(adj, axis=1)
            dinv = jnp.where(deg > 0, deg ** (-0.5), 0.0).astype(adj.dtype)
            return dinv[:, None] * adj * dinv[None, :]
        A_c = jax.lax.stop_gradient(A)
        adj = adjacent_mat((A_c + A_c.T) * 0.5)
        y = Coefficient2 @ adj
        y = y @ x
        return y
    x = _layernorm(x + _L0_gnn_ref(x, adj, adj), axis=-1)
    return x

_drawn_inputs = setup_inputs


def setup_inputs(seed=0):
    import zlib

    import numpy as np

    out = dict(_drawn_inputs(seed))
    spreads = {}
    factors = {}
    for name, (base, spread) in spreads.items():
        noise = np.random.default_rng([zlib.crc32(name.encode()), seed]).standard_normal(out[name].shape)
        drawn = base * np.exp(spread * noise) if base else spread * noise
        out[name] = jnp.asarray(drawn.astype(out[name].dtype))
    for name, factor in factors.items():
        out[name] = (out[name] * factor).astype(out[name].dtype)
    return out
```

```python
import concourse.bass as bass
from concourse import mybir
from contextlib import ExitStack


def gcn_residual_layernorm_kernel(nc: bass.Bass, x: bass.AP, adj: bass.AP, out: bass.AP):
    fp32 = mybir.dt.float32
    f32r = mybir.dt.float32r
    ALU = mybir.AluOpType
    ACT = mybir.ActivationFunctionType

    P = 128
    N, D = x.shape
    NT = (N + P - 1) // P
    TAIL = N - (NT - 1) * P
    FULL = NT - 1
    G1 = 6
    G2 = NT - G1
    SW = G1 * P
    NBANK = 8
    TRB = (6, 7)
    NSPLIT = 4
    NX = 4
    EPS = 1e-5
    TINY = 1.17549435e-38
    TR = 4

    def rows(t):
        return TAIL if t == NT - 1 else P

    def bank2(m):
        return (6, 7, 0, 1, 2)[m - G1]

    def bank3(i):
        return (3 + i) % NBANK

    chunks = []
    chunks_after = []
    rowchunks_after = []
    for k in range(NT):
        for i in range(k, NT, TR):
            chunks.append(("row", k, i, min(i + TR, NT)))
        rowchunks_after.append(len(chunks))
        for i in range(k + 1, NT, TR):
            chunks.append(("col", k, i, min(i + TR, NT)))
        chunks_after.append(len(chunks))

    def step_chunks(k):
        return range(chunks_after[k - 1] if k else 0, chunks_after[k])

    N1, N2 = NT, 2 * NT
    NN = N2 + 2 * NT

    def split_half(n):
        i, h = divmod(n - N2, 2)
        return i, (0, G1) if h == 0 else (G1, NT)

    ctx = ExitStack()
    with ctx:
        def sb(name, shape, dt=fp32):
            return ctx.enter_context(nc.sbuf_tensor(name, shape, dt))

        def sem(name):
            return ctx.enter_context(nc.semaphore(name))

        A = sb("A", [P, NT, N])
        AT = sb("AT", [P, NT, N])
        w_hi = sb("w_hi", [P, NSPLIT, SW], f32r)
        w_lo = sb("w_lo", [P, NSPLIT, SW], f32r)
        v_hi = sb("v_hi", [P, NT, D], f32r)
        v_lo = sb("v_lo", [P, NT, D], f32r)
        xs = sb("xs", [P, NX, D])
        ident = sb("ident", [P, P])
        ident2 = sb("ident2", [P, P])
        deg2 = sb("deg2", [P, NT])
        degc = sb("degc", [P, NT])
        power = sb("power", [P, NT])
        dinv = sb("dinv", [P, NT])
        dinvh = sb("dinvh", [P, NT])
        mhalf = sb("mhalf", [P, 1])
        stats = sb("stats", [P, NT, 6])
        mv = sb("mv", [P, NT, 2])
        veps = sb("veps", [P, NT])
        rstd = sb("rstd", [P, NT])
        bank = [ctx.enter_context(nc.psum_tensor(f"bank{b}", [P, 512], fp32)) for b in range(NBANK)]

        strip_here = [sem(f"strip_here{k}") for k in range(NT)]
        tail_here = sem("tail_here")
        x_here = [sem(f"x_here{s}") for s in range(NX)]
        consts = sem("consts")
        fills = sem("fills")
        tr_done = sem("tr_done")
        tr_out = sem("tr_out")
        diag_done = sem("diag_done")
        s_done = sem("s_done")
        degc_done = sem("degc_done")
        pow_done = sem("pow_done")
        dinv_done = sem("dinv_done")
        hi_done = sem("hi_done")
        lo_done = sem("lo_done")
        z_hi = sem("z_hi")
        z_lo = sem("z_lo")
        mm_done = sem("mm_done")
        acc_done = sem("acc_done")
        dinvh_done = sem("dinvh_done")
        u_raw = sem("u_raw")
        u_hi = sem("u_hi")
        u_lo = sem("u_lo")
        res_done = sem("res_done")
        st_done = sem("st_done")
        ag_done = sem("ag_done")
        ve_done = sem("ve_done")
        rs_done = sem("rs_done")
        ln_done = sem("ln_done")
        out_done = [sem(f"out_done{s}") for s in range(NX)]

        block = ctx.enter_context(nc.Block())

        def wait_acc(eng, m):
            if m == G1 - 1:
                eng.wait_ge(mm_done, N1)
            elif m == NT - 1:
                eng.wait_ge(mm_done, N2)
            else:
                eng.wait_ge(acc_done, m + 1 if m < G1 else m)

        @block.sync
        def _(sp):
            def load_x(n):
                t = n % NT
                if n >= NX:
                    if n - NX < NT:
                        sp.wait_ge(z_hi, n - NX + 1)
                        sp.wait_ge(z_lo, n - NX + 1)
                    else:
                        j = n - NX - NT
                        sp.wait_ge(out_done[(n - NX) % NX], 16 * ((j // NX) + 1))
                sp.dma_start(xs[:rows(t), n % NX, :], x[t * P:t * P + rows(t), :]).then_inc(x_here[n % NX], 16)

            for k in range(NT):
                r, c = k * P, (k + 1) * P
                if k < FULL:
                    sp.dma_start(A[:, k, r:N], adj[r:c, r:N]).then_inc(strip_here[k], 16)
                if k + 1 < FULL:
                    sp.dma_start(A[:, k + 1:FULL, r:c],
                                 adj[c:FULL * P, r:c].rearrange("(t p) c -> p t c", p=P)).then_inc(strip_here[k], 16)
                if k == 0:
                    sp.dma_start(A[0:64, FULL, :], adj[FULL * P:FULL * P + 64, :]).then_inc(tail_here, 16)
                    sp.dma_start(A[64:TAIL, FULL, :], adj[FULL * P + 64:N, :]).then_inc(tail_here, 16)
                load_x(k)
            for n in range(NT, NT + NX):
                load_x(n)
            for i in range(NT):
                s = (NT + i) % NX
                sp.wait_ge(ln_done, i + 1)
                sp.dma_start(out[i * P:i * P + rows(i), :], xs[:rows(i), s, :]).then_inc(out_done[s], 16)
                if i + NX < NT:
                    load_x(NT + i + NX)
            for s in range(NX):
                sp.wait_ge(out_done[s], 16 * sum((NT + i) % NX == s for i in range(NT)))

        @block.gpsimd
        def _(pool):
            nc.gpsimd.memset(ident[:], 0.0).then_inc(fills, 1)
            nc.gpsimd.memset(ident2[:], 0.0).then_inc(fills, 1)
            pool.wait_ge(fills, 2)
            nc.gpsimd.affine_select(out=ident[:], in_=ident[:], compare_op=ALU.not_equal, fill=1.0, base=0,
                                    pattern=[[-1, P]], channel_multiplier=1).then_inc(consts, 1)
            nc.gpsimd.affine_select(out=ident2[:], in_=ident2[:], compare_op=ALU.not_equal, fill=2.0, base=0,
                                    pattern=[[-1, P]], channel_multiplier=1).then_inc(consts, 1)
            nc.gpsimd.memset(mhalf[:], -0.5).then_inc(consts, 1)
            pool.wait_ge(consts, 3)
            nc.gpsimd.memset(AT[64:P, FULL, :], 0.0).then_inc(consts, 1)
            pool.wait_ge(consts, 4)
            for k in range(NT):
                p, r = rows(k), k * P
                pool.wait_ge(tr_done, (chunks_after[k - 1] if k else 0) + 1)
                nc.gpsimd.tensor_tensor(A[:p, k, r:r + p], A[:p, k, r:r + p], ident2[:p, :p],
                                        ALU.add).then_inc(diag_done, 1)
                pool.wait_ge(degc_done, k + 1)
                nc.gpsimd.tensor_tensor(power[:p, k:k + 1], degc[:p, k:k + 1], mhalf[:p, :],
                                        ALU.pow).then_inc(pow_done, 1)
            for i in range(NT):
                p = rows(i)
                pool.wait_ge(ve_done, i + 1)
                nc.gpsimd.tensor_tensor(rstd[:p, i:i + 1], veps[:p, i:i + 1], mhalf[:p, :],
                                        ALU.pow).then_inc(rs_done, 1)

        def split_source(n):
            if n < N1:
                return A[:rows(n), n, 0:SW], rows(n), SW
            if n < N2:
                k = n - N1
                return A[:rows(k), k, SW:N], rows(k), N - SW
            i, (k0, k1) = split_half(n)
            return AT[:, k0:k1, i * P:i * P + rows(i)], P, (k1 - k0) * rows(i)

        def slot(w, n):
            src, p, width = split_source(n)
            dst = w[:p, n % NSPLIT, 0:width]
            if n >= N2:
                dst = dst.rearrange("p (k c) -> p k c", c=rows(split_half(n)[0]))
            return dst

        @block.scalar
        def _(act):
            def hi(n):
                if n < N1:
                    act.wait_ge(s_done, n + 1)
                if n >= NSPLIT:
                    act.wait_ge(mm_done, n - NSPLIT + 1)
                nc.scalar.activation(slot(w_hi, n), split_source(n)[0], ACT.Copy).then_inc(hi_done, 1)

            def u_high(m):
                act.wait_ge(mm_done, N1 + m + 1)
                if m < G1:
                    act.wait_ge(u_raw, m + 1)
                    nc.scalar.activation(v_hi[:, m, :], A[:, m, 0:D], ACT.Copy).then_inc(u_hi, 1)
                else:
                    p = rows(m)
                    wait_acc(act, m)
                    nc.scalar.activation(v_hi[:p, m, :], bank[bank2(m)][:p, :], ACT.Copy,
                                         scale=dinvh[:p, m:m + 1]).then_inc(u_hi, 1)

            act.wait_ge(consts, 4)
            for k in range(NT):
                for c in step_chunks(k):
                    kind, _, i0, i1 = chunks[c]
                    act.wait_ge(tr_done, c + 1)
                    src = bank[TRB[c % 2]]
                    if kind == "row":
                        w = min(i1 * P, N) - i0 * P
                        nc.scalar.activation(AT[:rows(k), k, i0 * P:i0 * P + w], src[:rows(k), 0:w],
                                             ACT.Copy).then_inc(tr_out, 1)
                        continue
                    r = rows(k)
                    full = min(i1, FULL)
                    if full > i0:
                        ins = nc.scalar.activation(AT[:, i0:full, k * P:(k + 1) * P],
                                                   src[:, 0:(full - i0) * P].rearrange("p (t c) -> p t c", c=P),
                                                   ACT.Copy)
                    if i1 == NT:
                        ins = nc.scalar.activation(AT[:TAIL, FULL, k * P:(k + 1) * P],
                                                   src[:TAIL, (FULL - i0) * P:(NT - i0) * P], ACT.Copy)
                    ins.then_inc(tr_out, 1)
                hi(k)
                p = rows(k)
                act.wait_ge(dinv_done, k + 1)
                act.wait_ge(x_here[k % NX], 16 * (k // NX + 1))
                nc.scalar.activation(v_hi[:p, k, :], xs[:p, k % NX, :], ACT.Copy,
                                     scale=dinv[:p, k:k + 1]).then_inc(z_hi, 1)
            for n in range(N1, N1 + 3):
                hi(n)
            act.wait_ge(dinvh_done, NT)
            for m in range(G1):
                wait_acc(act, m)
                nc.scalar.activation(A[:, m, 0:D], bank[m][:, :], ACT.Copy,
                                     scale=dinvh[:, m:m + 1]).then_inc(u_raw, 1)
            hi(N1 + 3)
            for n in range(N1 + 4, N2 + 3):
                hi(n)
                if n - N1 - 4 < G1:
                    u_high(n - N1 - 4)
            for m in range(G1, NT):
                u_high(m)
            for n in range(N2 + 3, NN):
                hi(n)

        @block.vector
        def _(dve):
            def lo(n):
                dve.wait_ge(hi_done, n + 1)
                if n >= NSPLIT:
                    dve.wait_ge(mm_done, n - NSPLIT + 1)
                nc.vector.tensor_tensor(slot(w_lo, n), split_source(n)[0], slot(w_hi, n).bitcast(fp32),
                                        ALU.subtract).then_inc(lo_done, 1)

            def u_low(m):
                p = rows(m)
                dve.wait_ge(u_hi, m + 1)
                if m < G1:
                    nc.vector.tensor_tensor(v_lo[:, m, :], A[:, m, 0:D], v_hi[:, m, :].bitcast(fp32),
                                            ALU.subtract).then_inc(u_lo, 1)
                else:
                    nc.vector.scalar_tensor_tensor(v_lo[:p, m, :], bank[bank2(m)][:p, :], dinvh[:p, m:m + 1],
                                                   v_hi[:p, m, :].bitcast(fp32), ALU.mult,
                                                   ALU.subtract).then_inc(u_lo, 1)

            def finish(i):
                p, s = rows(i), (NT + i) % NX
                dve.wait_ge(mm_done, N2 + 2 * i + 2)
                dve.wait_ge(x_here[s], 16 * ((NT + i) // NX + 1))
                nc.vector.tensor_tensor(xs[:p, s, :], bank[bank3(i)][:p, :], xs[:p, s, :],
                                        ALU.add).then_inc(res_done, 1)
                dve.wait_ge(res_done, i + 1)
                nc.vector.bn_stats(stats[:p, i, :], xs[:p, s, :]).then_inc(st_done, 1)
                dve.wait_ge(st_done, i + 1)
                nc.vector.bn_aggr(mv[:p, i, :], stats[:p, i, :]).then_inc(ag_done, 1)
                dve.wait_ge(ag_done, i + 1)
                nc.vector.tensor_scalar(veps[:p, i:i + 1], mv[:p, i, 1:2], EPS, None, ALU.add).then_inc(ve_done, 1)
                dve.wait_ge(rs_done, i + 1)
                nc.vector.tensor_scalar(xs[:p, s, :], xs[:p, s, :], mv[:p, i, 0:1], rstd[:p, i:i + 1],
                                        ALU.subtract, ALU.mult).then_inc(ln_done, 1)

            for k in range(NT):
                p = rows(k)
                dve.wait_ge(tr_out, rowchunks_after[k])
                dve.wait_ge(diag_done, k + 1)
                dve.wait_ge(tr_done, chunks_after[k])
                nc.vector.scalar_tensor_tensor(A[:p, k, :], A[:p, k, :], 1.0, AT[:p, k, :], ALU.mult, ALU.add,
                                               accum_out=deg2[:p, k:k + 1]).then_inc(s_done, 1)
                dve.wait_ge(s_done, k + 1)
                nc.vector.tensor_scalar(degc[:p, k:k + 1], deg2[:p, k:k + 1], 0.5, TINY, ALU.mult,
                                        ALU.max).then_inc(degc_done, 1)
                lo(k)
                dve.wait_ge(pow_done, k + 1)
                nc.vector.scalar_tensor_tensor(dinv[:p, k:k + 1], deg2[:p, k:k + 1], 0.0, power[:p, k:k + 1],
                                               ALU.is_gt, ALU.mult).then_inc(dinv_done, 1)
                dve.wait_ge(z_hi, k + 1)
                nc.vector.scalar_tensor_tensor(v_lo[:p, k, :], xs[:p, k % NX, :], dinv[:p, k:k + 1],
                                               v_hi[:p, k, :].bitcast(fp32), ALU.mult, ALU.subtract).then_inc(z_lo, 1)
                nc.vector.tensor_scalar(dinvh[:p, k:k + 1], dinv[:p, k:k + 1], 0.5, None,
                                        ALU.mult).then_inc(dinvh_done, 1)
            dve.wait_ge(dinvh_done, NT)
            for n in range(N1, N1 + 4):
                lo(n)
            for n in range(N1 + 4, N2 + 3):
                lo(n)
                if n - N1 - 4 < G1:
                    u_low(n - N1 - 4)
            for m in range(G1, NT):
                u_low(m)
            done = 0
            for n in range(N2 + 3, NN):
                lo(n)
                if (n - N2) % 2 == 0:
                    finish(done)
                    done += 1
            while done < NT:
                finish(done)
                done += 1

        @block.tensor
        def _(pe):
            def transposes(c):
                kind, k, i0, i1 = chunks[c]
                if c >= 2:
                    pe.wait_ge(tr_out, c - 1)
                dst = bank[TRB[c % 2]]
                for i in range(i0, i1):
                    at = (i - i0) * P
                    if kind == "row":
                        src, p, w = A[:rows(i), i, k * P:k * P + rows(k)], rows(k), rows(i)
                    else:
                        src, p, w = A[:rows(k), k, i * P:i * P + rows(i)], rows(i), rows(k)
                    last = nc.tensor.transpose(dst[:p, at:at + w], src, ident[:w, :w])
                last.then_inc(tr_done, 1)

            def product(n, dst, col, k, first, last):
                p, m = rows(k), dst.shape[0]
                hi = w_hi[:p, n % NSPLIT, col:col + m]
                lo = w_lo[:p, n % NSPLIT, col:col + m]
                nc.tensor.matmul(dst, lo, v_hi[:p, k, :], start=first, stop=False)
                nc.tensor.matmul(dst, hi, v_lo[:p, k, :], start=False, stop=False)
                return nc.tensor.matmul(dst, hi, v_hi[:p, k, :], start=False, stop=last)

            def step_transposes(k):
                if k < FULL:
                    pe.wait_ge(strip_here[k], 32 if k + 1 < FULL else 16)
                return list(step_chunks(k))

            pe.wait_ge(consts, 1)
            for k in range(2):
                todo = step_transposes(k)
                if k == 0:
                    pe.wait_ge(tail_here, 32)
                for c in todo:
                    transposes(c)
            for k in range(NT):
                todo = step_transposes(k + 2) if k + 2 < NT else []
                pe.wait_ge(hi_done, k + 1)
                pe.wait_ge(lo_done, k + 1)
                pe.wait_ge(z_hi, k + 1)
                pe.wait_ge(z_lo, k + 1)
                for m in range(G1):
                    if todo:
                        transposes(todo.pop(0))
                    ins = product(k, bank[m][:, :], m * P, k, k == 0, k == NT - 1)
                    if k == NT - 1 and m < G1 - 1:
                        ins.then_inc(acc_done, 1)
                ins.then_inc(mm_done, 1)
            for k in range(NT):
                n = N1 + k
                pe.wait_ge(hi_done, n + 1)
                pe.wait_ge(lo_done, n + 1)
                for m in range(G1, NT):
                    if k == 0:
                        if bank2(m) in TRB:
                            pe.wait_ge(tr_out, len(chunks))
                        else:
                            pe.wait_ge(u_raw, bank2(m) + 1)
                    ins = product(n, bank[bank2(m)][:rows(m), :], (m - G1) * P, k, k == 0, k == NT - 1)
                    if k == NT - 1 and m < NT - 1:
                        ins.then_inc(acc_done, 1)
                ins.then_inc(mm_done, 1)
            for n in range(N2, NN):
                i, (k0, k1) = split_half(n)
                pe.wait_ge(hi_done, n + 1)
                pe.wait_ge(lo_done, n + 1)
                if k0 == 0:
                    if bank3(i) in (3, 4, 5) and i < NBANK:
                        pe.wait_ge(u_raw, bank3(i) + 1)
                    elif i < NBANK:
                        pe.wait_ge(u_lo, NT)
                    else:
                        pe.wait_ge(res_done, i - NBANK + 1)
                for k in range(k0, k1):
                    if i == 0:
                        pe.wait_ge(u_lo, k + 1)
                    ins = product(n, bank[bank3(i)][:rows(i), :], (k - k0) * rows(i), k, k == 0, k == NT - 1)
                ins.then_inc(mm_done, 1)


_INS = ["x", "adj"]


def kernel(**inputs):
    import numpy as _np
    import concourse.bacc as _bacc
    from concourse import mybir as _mybir
    from concourse.bass_utils import run_bass_kernel_spmd as _run

    nc = _bacc.Bacc("TRN2", target_bir_lowering=False, num_devices=1)
    arrays, args = {}, []
    for name in _INS:
        a = _np.ascontiguousarray(inputs[name])
        arrays[f"in_{name}"] = a
        args.append(nc.dram_tensor(f"in_{name}", a.shape, _mybir.dt.from_np(a.dtype), kind="ExternalInput").ap())
    shape = inputs["x"].shape
    args.append(nc.dram_tensor("out", shape, _mybir.dt.from_np(_np.dtype("float32")), kind="ExternalOutput").ap())
    gcn_residual_layernorm_kernel(nc, *args)
    r = _run(nc, [arrays], core_ids=[0])
    return r.results[0]["out"]
```

```python
import concourse.bass as bass
from concourse import mybir
from contextlib import ExitStack


def gcn_residual_layernorm_kernel(nc: bass.Bass, x: bass.AP, adj: bass.AP, out: bass.AP):
    fp32 = mybir.dt.float32
    f32r = mybir.dt.float32r
    ALU = mybir.AluOpType
    ACT = mybir.ActivationFunctionType

    P = 128
    N, D = x.shape
    NT = (N + P - 1) // P
    TAIL = N - (NT - 1) * P
    FULL = NT - 1
    G1 = 6
    G2 = NT - G1
    SW = G1 * P
    NBANK = 8
    TRB = (6, 7)
    NSPLIT = 4
    NX = 4
    EPS = 1e-5
    WARM, WARM2 = 5, 8
    AHEAD = 2
    TINY = 1.17549435e-38
    TR = 4

    def rows(t):
        return TAIL if t == NT - 1 else P

    def bank2(m):
        return (6, 7, 0, 1, 2)[m - G1]

    def bank3(i):
        return (3 + i) % NBANK

    chunks = []
    chunks_after = []
    rowchunks_after = []
    for k in range(NT):
        cuts = sorted({*range(k, NT, TR)} if k else {*range(0, G1, TR), *range(G1, NT, TR)}) + [NT]
        for i0, i1 in zip(cuts, cuts[1:]):
            chunks.append(("row", k, i0, i1))
        rowchunks_after.append(len(chunks))
        for i in range(k + 1, NT, TR):
            chunks.append(("col", k, i, min(i + TR, NT)))
        chunks_after.append(len(chunks))

    def step_chunks(k):
        return range(chunks_after[k - 1] if k else 0, chunks_after[k])

    N1, N2 = NT, 2 * NT
    NN = N2 + 2 * NT

    def split_half(n):
        i, h = divmod(n - N2, 2)
        return i, (0, G1) if h == 0 else (G1, NT)

    ctx = ExitStack()
    with ctx:
        def sb(name, shape, dt=fp32):
            return ctx.enter_context(nc.sbuf_tensor(name, shape, dt))

        def sem(name):
            return ctx.enter_context(nc.semaphore(name))

        A = sb("A", [P, NT, N])
        S = sb("S", [P, 2, N])
        AT = sb("AT", [P, NT, N])
        w_hi = sb("w_hi", [P, NSPLIT, SW], f32r)
        w_lo = sb("w_lo", [P, NSPLIT, SW], f32r)
        v_hi = sb("v_hi", [P, NT, D], f32r)
        v_lo = sb("v_lo", [P, NT, D], f32r)
        xs = sb("xs", [P, NX, D])
        ident = sb("ident", [P, P])
        ident2 = sb("ident2", [P, P])
        sums = sb("sums", [P, NT, 2])
        deg2 = sb("deg2", [P, NT])
        degc = sb("degc", [P, NT])
        power = sb("power", [P, NT])
        dinv = sb("dinv", [P, NT])
        dinvh = sb("dinvh", [P, NT])
        mhalf = sb("mhalf", [P, 1])
        stats = sb("stats", [P, NT, 6])
        mv = sb("mv", [P, NT, 2])
        veps = sb("veps", [P, NT])
        rstd = sb("rstd", [P, NT])
        bank = [ctx.enter_context(nc.psum_tensor(f"bank{b}", [P, 512], fp32)) for b in range(NBANK)]

        strip_here = [sem(f"strip_here{k}") for k in range(NT)]
        first_here = [sem(f"first_here{j}") for j in range(4)]
        tail_here = sem("tail_here")
        warm_done = sem("warm_done")
        kept = sem("kept")
        deg_done = sem("deg_done")
        x_here = [sem(f"x_here{s}") for s in range(NX)]
        consts = sem("consts")
        fills = sem("fills")
        tr_done = sem("tr_done")
        tr_out = sem("tr_out")
        diag_done = sem("diag_done")
        s_done = sem("s_done")
        degc_done = sem("degc_done")
        pow_done = sem("pow_done")
        dinv_done = sem("dinv_done")
        hi_done = sem("hi_done")
        lo_done = sem("lo_done")
        z_hi = sem("z_hi")
        z_lo = sem("z_lo")
        mm_done = sem("mm_done")
        acc_done = sem("acc_done")
        dinvh_done = sem("dinvh_done")
        u_raw = sem("u_raw")
        u_hi = sem("u_hi")
        u_lo = sem("u_lo")
        res_done = sem("res_done")
        st_done = sem("st_done")
        ag_done = sem("ag_done")
        ve_done = sem("ve_done")
        rs_done = sem("rs_done")
        ln_done = sem("ln_done")
        out_done = [sem(f"out_done{s}") for s in range(NX)]

        block = ctx.enter_context(nc.Block())

        def wait_acc(eng, m):
            if m == G1 - 1:
                eng.wait_ge(mm_done, N1)
            elif m == NT - 1:
                eng.wait_ge(mm_done, N2)
            else:
                eng.wait_ge(acc_done, m + 1 if m < G1 else m)

        @block.sync
        def _(sp):
            def load_x(n):
                t = n % NT
                if n >= NX:
                    if n - NX < NT:
                        sp.wait_ge(z_hi, n - NX + 1)
                        sp.wait_ge(z_lo, n - NX + 1)
                    else:
                        j = n - NX - NT
                        sp.wait_ge(out_done[(n - NX) % NX], 16 * ((j // NX) + 1))
                sp.dma_start(xs[:rows(t), n % NX, :], x[t * P:t * P + rows(t), :]).then_inc(x_here[n % NX], 16)

            def blocks(t0, t1):
                return A[:, t0:t1, 0:P], adj[t0 * P:t1 * P, 0:P].rearrange("(t p) c -> p t c", p=P)

            sp.dma_start(*blocks(0, TR)).then_inc(first_here[0], 16)
            sp.dma_start(*blocks(TR, G1)).then_inc(first_here[1], 16)
            sp.dma_start(A[:, 0, P:SW], adj[0:P, P:SW]).then_inc(first_here[1], 16)
            sp.dma_start(*blocks(G1, FULL)).then_inc(first_here[2], 16)
            sp.dma_start(A[0:64, FULL, 0:P], adj[FULL * P:FULL * P + 64, 0:P]).then_inc(first_here[3], 16)
            sp.dma_start(A[64:TAIL, FULL, 0:P], adj[FULL * P + 64:N, 0:P]).then_inc(first_here[3], 16)
            sp.dma_start(A[:, 0, SW:N], adj[0:P, SW:N]).then_inc(first_here[3], 16)
            load_x(0)
            for k in range(1, NT):
                r, c = k * P, (k + 1) * P
                if k == 1:
                    sp.dma_start(A[0:64, FULL, P:N], adj[FULL * P:FULL * P + 64, P:N]).then_inc(tail_here, 16)
                    sp.dma_start(A[64:TAIL, FULL, P:N], adj[FULL * P + 64:N, P:N]).then_inc(tail_here, 16)
                if k < FULL:
                    sp.dma_start(A[:, k, r:N], adj[r:c, r:N]).then_inc(strip_here[k], 16)
                if k + 1 < FULL:
                    sp.dma_start(A[:, k + 1:FULL, r:c],
                                 adj[c:FULL * P, r:c].rearrange("(t p) c -> p t c", p=P)).then_inc(strip_here[k], 16)
                load_x(k)
            for n in range(NT, NT + NX):
                load_x(n)
            for i in range(NT):
                s = (NT + i) % NX
                sp.wait_ge(ln_done, i + 1)
                sp.dma_start(out[i * P:i * P + rows(i), :], xs[:rows(i), s, :]).then_inc(out_done[s], 16)
                if i + NX < NT:
                    load_x(NT + i + NX)
            for s in range(NX):
                sp.wait_ge(out_done[s], 16 * sum((NT + i) % NX == s for i in range(NT)))

        @block.gpsimd
        def _(pool):
            nc.gpsimd.memset(ident[:], 0.0).then_inc(fills, 1)
            nc.gpsimd.memset(ident2[:], 0.0).then_inc(fills, 1)
            pool.wait_ge(fills, 2)
            nc.gpsimd.affine_select(out=ident[:], in_=ident[:], compare_op=ALU.not_equal, fill=1.0, base=0,
                                    pattern=[[-1, P]], channel_multiplier=1).then_inc(consts, 1)
            nc.gpsimd.affine_select(out=ident2[:], in_=ident2[:], compare_op=ALU.not_equal, fill=2.0, base=0,
                                    pattern=[[-1, P]], channel_multiplier=1).then_inc(consts, 1)
            nc.gpsimd.memset(mhalf[:], -0.5).then_inc(consts, 1)
            pool.wait_ge(consts, 3)
            nc.gpsimd.memset(AT[64:P, FULL, :], 0.0).then_inc(consts, 1)
            pool.wait_ge(consts, 4)
            for k in range(NT):
                p, r = rows(k), k * P
                pool.wait_ge(tr_done, (chunks_after[k - 1] if k else 0) + 1)
                nc.gpsimd.tensor_tensor(A[:p, k, r:r + p], A[:p, k, r:r + p], ident2[:p, :p],
                                        ALU.add).then_inc(diag_done, 1)
                pool.wait_ge(degc_done, k + 1)
                nc.gpsimd.tensor_tensor(power[:p, k:k + 1], degc[:p, k:k + 1], mhalf[:p, :],
                                        ALU.pow).then_inc(pow_done, 1)
            for i in range(NT):
                p = rows(i)
                pool.wait_ge(ve_done, i + 1)
                nc.gpsimd.tensor_tensor(rstd[:p, i:i + 1], veps[:p, i:i + 1], mhalf[:p, :],
                                        ALU.pow).then_inc(rs_done, 1)

        def split_source(n):
            if n < N1:
                return S[:rows(n), n % 2, 0:SW], rows(n), SW
            if n < N2:
                k = n - N1
                return A[:rows(k), k, SW:N], rows(k), N - SW
            i, (k0, k1) = split_half(n)
            return AT[:, k0:k1, i * P:i * P + rows(i)], P, (k1 - k0) * rows(i)

        def slot(w, n):
            src, p, width = split_source(n)
            dst = w[:p, n % NSPLIT, 0:width]
            if n >= N2:
                dst = dst.rearrange("p (k c) -> p k c", c=rows(split_half(n)[0]))
            return dst

        @block.scalar
        def _(act):
            def hi(n):
                if n < N1:
                    act.wait_ge(s_done, 2 * n + 1)
                elif n < N2:
                    act.wait_ge(kept, n - N1 + 1)
                if n >= NSPLIT:
                    act.wait_ge(mm_done, n - NSPLIT + 1)
                nc.scalar.activation(slot(w_hi, n), split_source(n)[0], ACT.Copy).then_inc(hi_done, 1)

            def u_high(m):
                act.wait_ge(mm_done, N1 + m + 1)
                if m < G1:
                    act.wait_ge(u_raw, m + 1)
                    nc.scalar.activation(v_hi[:, m, :], A[:, m, 0:D], ACT.Copy).then_inc(u_hi, 1)
                else:
                    p = rows(m)
                    wait_acc(act, m)
                    nc.scalar.activation(v_hi[:p, m, :], bank[bank2(m)][:p, :], ACT.Copy,
                                         scale=dinvh[:p, m:m + 1]).then_inc(u_hi, 1)

            def evacuate(c):
                kind, k, i0, i1 = chunks[c]
                act.wait_ge(tr_done, c + 1)
                src = bank[TRB[c % 2]]
                if kind == "row":
                    w = min(i1 * P, N) - i0 * P
                    nc.scalar.activation(AT[:rows(k), k, i0 * P:i0 * P + w], src[:rows(k), 0:w],
                                         ACT.Copy).then_inc(tr_out, 1)
                    return
                full = min(i1, FULL)
                if full > i0:
                    ins = nc.scalar.activation(AT[:, i0:full, k * P:(k + 1) * P],
                                               src[:, 0:(full - i0) * P].rearrange("p (t c) -> p t c", c=P),
                                               ACT.Copy)
                if i1 == NT:
                    ins = nc.scalar.activation(AT[:TAIL, FULL, k * P:(k + 1) * P],
                                               src[:TAIL, (FULL - i0) * P:(NT - i0) * P], ACT.Copy)
                ins.then_inc(tr_out, 1)

            act.wait_ge(consts, 4)
            nc.scalar.activation(AT[:, 0, 0:1], ident[:, 0:1], ACT.Copy).then_inc(warm_done, 1)
            act.wait_ge(warm_done, 1)
            for k in range(NT):
                cols = range(rowchunks_after[k], chunks_after[k])
                if k < 3:
                    for c in range(chunks_after[k - 1] if k else 0, rowchunks_after[k]):
                        evacuate(c)
                for c in cols[:1 if k else 0]:
                    evacuate(c)
                hi(k)
                for c in cols[1 if k else 0:]:
                    evacuate(c)
                if 2 <= k < NT - 1:
                    for c in range(chunks_after[k], rowchunks_after[k + 1]):
                        evacuate(c)
                p = rows(k)
                act.wait_ge(dinv_done, k + 1)
                act.wait_ge(x_here[k % NX], 16 * (k // NX + 1))
                nc.scalar.activation(v_hi[:p, k, :], xs[:p, k % NX, :], ACT.Copy,
                                     scale=dinv[:p, k:k + 1]).then_inc(z_hi, 1)
                nc.scalar.activation(A[:p, k, SW:N], S[:p, k % 2, SW:N], ACT.Copy).then_inc(kept, 1)
            for n in range(N1, N1 + 3):
                hi(n)
            act.wait_ge(dinvh_done, NT)
            for m in range(G1):
                wait_acc(act, m)
                nc.scalar.activation(A[:, m, 0:D], bank[m][:, :], ACT.Copy,
                                     scale=dinvh[:, m:m + 1]).then_inc(u_raw, 1)
            hi(N1 + 3)
            for n in range(N1 + 4, N2 + 3):
                hi(n)
                if n - N1 - 4 < G1:
                    u_high(n - N1 - 4)
            for m in range(G1, NT):
                u_high(m)
            for n in range(N2 + 3, NN):
                hi(n)

        @block.vector
        def _(dve):
            def lo(n):
                dve.wait_ge(hi_done, n + 1)
                if n >= NSPLIT:
                    dve.wait_ge(mm_done, n - NSPLIT + 1)
                nc.vector.tensor_tensor(slot(w_lo, n), split_source(n)[0], slot(w_hi, n).bitcast(fp32),
                                        ALU.subtract).then_inc(lo_done, 1)

            def u_low(m):
                p = rows(m)
                dve.wait_ge(u_hi, m + 1)
                if m < G1:
                    nc.vector.tensor_tensor(v_lo[:, m, :], A[:, m, 0:D], v_hi[:, m, :].bitcast(fp32),
                                            ALU.subtract).then_inc(u_lo, 1)
                else:
                    nc.vector.scalar_tensor_tensor(v_lo[:p, m, :], bank[bank2(m)][:p, :], dinvh[:p, m:m + 1],
                                                   v_hi[:p, m, :].bitcast(fp32), ALU.mult,
                                                   ALU.subtract).then_inc(u_lo, 1)

            def finish(i):
                p, s = rows(i), (NT + i) % NX
                dve.wait_ge(mm_done, N2 + 2 * i + 2)
                dve.wait_ge(x_here[s], 16 * ((NT + i) // NX + 1))
                nc.vector.tensor_tensor(xs[:p, s, :], bank[bank3(i)][:p, :], xs[:p, s, :],
                                        ALU.add).then_inc(res_done, 1)
                dve.wait_ge(res_done, i + 1)
                nc.vector.bn_stats(stats[:p, i, :], xs[:p, s, :]).then_inc(st_done, 1)
                dve.wait_ge(st_done, i + 1)
                nc.vector.bn_aggr(mv[:p, i, :], stats[:p, i, :]).then_inc(ag_done, 1)
                dve.wait_ge(ag_done, i + 1)
                nc.vector.tensor_scalar(veps[:p, i:i + 1], mv[:p, i, 1:2], EPS, None, ALU.add).then_inc(ve_done, 1)
                dve.wait_ge(rs_done, i + 1)
                nc.vector.tensor_scalar(xs[:p, s, :], xs[:p, s, :], mv[:p, i, 0:1], rstd[:p, i:i + 1],
                                        ALU.subtract, ALU.mult).then_inc(ln_done, 1)

            def form_s(k):
                p = rows(k)
                if k >= 2:
                    dve.wait_ge(kept, k - 1)
                for h, (c0, c1) in enumerate(((0, SW), (SW, N))):
                    if k == 0:
                        dve.wait_ge(tr_out, 2 if h == 0 else rowchunks_after[0])
                    else:
                        dve.wait_ge(tr_out, rowchunks_after[k])
                    dve.wait_ge(diag_done, k + 1)
                    if k == 0:
                        dve.wait_ge(first_here[1 + 2 * h], 32 + 16 * h)
                    nc.vector.scalar_tensor_tensor(S[:p, k % 2, c0:c1], A[:p, k, c0:c1], 1.0, AT[:p, k, c0:c1],
                                                   ALU.mult, ALU.add,
                                                   accum_out=sums[:p, k, h:h + 1]).then_inc(s_done, 1)

            for k in range(NT):
                p = rows(k)
                if k < 3:
                    form_s(k)
                dve.wait_ge(s_done, 2 * k + 2)
                nc.vector.tensor_tensor(deg2[:p, k:k + 1], sums[:p, k, 0:1], sums[:p, k, 1:2],
                                        ALU.add).then_inc(deg_done, 1)
                dve.wait_ge(deg_done, k + 1)
                nc.vector.tensor_scalar(degc[:p, k:k + 1], deg2[:p, k:k + 1], 0.5, TINY, ALU.mult,
                                        ALU.max).then_inc(degc_done, 1)
                lo(k)
                dve.wait_ge(pow_done, k + 1)
                nc.vector.scalar_tensor_tensor(dinv[:p, k:k + 1], deg2[:p, k:k + 1], 0.0, power[:p, k:k + 1],
                                               ALU.is_gt, ALU.mult).then_inc(dinv_done, 1)
                if 2 <= k < NT - 1:
                    form_s(k + 1)
                dve.wait_ge(z_hi, k + 1)
                nc.vector.scalar_tensor_tensor(v_lo[:p, k, :], xs[:p, k % NX, :], dinv[:p, k:k + 1],
                                               v_hi[:p, k, :].bitcast(fp32), ALU.mult, ALU.subtract).then_inc(z_lo, 1)
                nc.vector.tensor_scalar(dinvh[:p, k:k + 1], dinv[:p, k:k + 1], 0.5, None,
                                        ALU.mult).then_inc(dinvh_done, 1)
            dve.wait_ge(dinvh_done, NT)
            for n in range(N1, N1 + 4):
                lo(n)
            for n in range(N1 + 4, N2 + 3):
                lo(n)
                if n - N1 - 4 < G1:
                    u_low(n - N1 - 4)
            for m in range(G1, NT):
                u_low(m)
            done = 0
            for n in range(N2 + 3, NN):
                lo(n)
                if (n - N2) % 2 == 0:
                    finish(done)
                    done += 1
            while done < NT:
                finish(done)
                done += 1

        @block.tensor
        def _(pe):
            def transposes(c):
                kind, k, i0, i1 = chunks[c]
                if c >= 2:
                    pe.wait_ge(tr_out, c - 1)
                dst = bank[TRB[c % 2]]
                for i in range(i0, i1):
                    at = (i - i0) * P
                    if kind == "row":
                        src, p, w = A[:rows(i), i, k * P:k * P + rows(k)], rows(k), rows(i)
                    else:
                        src, p, w = A[:rows(k), k, i * P:i * P + rows(i)], rows(i), rows(k)
                    last = nc.tensor.transpose(dst[:p, at:at + w], src, ident[:w, :w])
                last.then_inc(tr_done, 1)

            def product(n, dst, col, k, first, last):
                p, m = rows(k), dst.shape[0]
                hi = w_hi[:p, n % NSPLIT, col:col + m]
                lo = w_lo[:p, n % NSPLIT, col:col + m]
                nc.tensor.matmul(dst, lo, v_hi[:p, k, :], start=first, stop=False)
                nc.tensor.matmul(dst, hi, v_lo[:p, k, :], start=False, stop=False)
                return nc.tensor.matmul(dst, hi, v_hi[:p, k, :], start=False, stop=last)

            def next_transposes():
                c = pending.pop(0)
                k = chunks[c][1]
                if c == chunks_after[k - 1]:
                    pe.wait_ge(strip_here[k], 32 if k + 1 < FULL else 16) if k < FULL else None
                    if k == 1:
                        pe.wait_ge(tail_here, 32)
                transposes(c)

            pe.wait_ge(consts, 1)
            def warm_up(n):
                for _ in range(n):
                    nc.tensor.matmul(bank[0][:, 0:P], ident[:, :], ident[:, :], start=True, stop=True)

            warm_up(WARM)
            for c in step_chunks(0):
                if c == 0:
                    pe.wait_ge(first_here[0], 16)
                elif c == 1:
                    pe.wait_ge(first_here[1], 32)
                elif c == 2:
                    pe.wait_ge(first_here[2], 16)
                elif c == 3:
                    pe.wait_ge(first_here[3], 48)
                transposes(c)
            pending = list(range(chunks_after[0], len(chunks)))
            warm_up(WARM2)
            for k in range(NT):
                if k == 1:
                    next_transposes()
                    next_transposes()
                pe.wait_ge(hi_done, k + 1)
                pe.wait_ge(lo_done, k + 1)
                pe.wait_ge(z_hi, k + 1)
                pe.wait_ge(z_lo, k + 1)
                for m in range(G1):
                    if pending and chunks[pending[0]][1] <= k + (AHEAD if k else 1):
                        next_transposes()
                    ins = product(k, bank[m][:, :], m * P, k, k == 0, k == NT - 1)
                    if k == NT - 1 and m < G1 - 1:
                        ins.then_inc(acc_done, 1)
                ins.then_inc(mm_done, 1)
            for k in range(NT):
                n = N1 + k
                pe.wait_ge(hi_done, n + 1)
                pe.wait_ge(lo_done, n + 1)
                for m in range(G1, NT):
                    if k == 0:
                        if bank2(m) in TRB:
                            pe.wait_ge(tr_out, len(chunks))
                        else:
                            pe.wait_ge(u_raw, bank2(m) + 1)
                    ins = product(n, bank[bank2(m)][:rows(m), :], (m - G1) * P, k, k == 0, k == NT - 1)
                    if k == NT - 1 and m < NT - 1:
                        ins.then_inc(acc_done, 1)
                ins.then_inc(mm_done, 1)
            for n in range(N2, NN):
                i, (k0, k1) = split_half(n)
                pe.wait_ge(hi_done, n + 1)
                pe.wait_ge(lo_done, n + 1)
                if k0 == 0:
                    if bank3(i) in (3, 4, 5) and i < NBANK:
                        pe.wait_ge(u_raw, bank3(i) + 1)
                    elif i < NBANK:
                        pe.wait_ge(u_lo, NT)
                    else:
                        pe.wait_ge(res_done, i - NBANK + 1)
                for k in range(k0, k1):
                    if i == 0:
                        pe.wait_ge(u_lo, k + 1)
                    ins = product(n, bank[bank3(i)][:rows(i), :], (k - k0) * rows(i), k, k == 0, k == NT - 1)
                ins.then_inc(mm_done, 1)


_INS = ["x", "adj"]


def kernel(**inputs):
    import numpy as _np
    import concourse.bacc as _bacc
    from concourse import mybir as _mybir
    from concourse.bass_utils import run_bass_kernel_spmd as _run

    nc = _bacc.Bacc("TRN2", target_bir_lowering=False, num_devices=1)
    arrays, args = {}, []
    for name in _INS:
        a = _np.ascontiguousarray(inputs[name])
        arrays[f"in_{name}"] = a
        args.append(nc.dram_tensor(f"in_{name}", a.shape, _mybir.dt.from_np(a.dtype), kind="ExternalInput").ap())
    shape = inputs["x"].shape
    args.append(nc.dram_tensor("out", shape, _mybir.dt.from_np(_np.dtype("float32")), kind="ExternalOutput").ap())
    gcn_residual_layernorm_kernel(nc, *args)
    r = _run(nc, [arrays], core_ids=[0])
    return r.results[0]["out"]
```

```python
import concourse.bass as bass
from concourse import mybir
from contextlib import ExitStack


def gcn_residual_layernorm_kernel(nc: bass.Bass, x: bass.AP, adj: bass.AP, out: bass.AP):
    fp32 = mybir.dt.float32
    f32r = mybir.dt.float32r
    ALU = mybir.AluOpType
    ACT = mybir.ActivationFunctionType

    P = 128
    N, D = x.shape
    NT = (N + P - 1) // P
    TAIL = N - (NT - 1) * P
    FULL = NT - 1
    G1 = 6
    SW = G1 * P
    NBANK = 8
    TRB = (6, 7)
    NSPLIT = 4
    NX = 4
    EPS = 1e-5
    WARM, WARM2 = 5, 6
    S_AHEAD = 3
    AHEAD = 2
    BIG = 1e38
    EARLY = 3
    TR = 4

    DUP1 = 48
    DUP2 = TAIL - DUP1
    PASS2 = [*range(FULL - 1), FULL, FULL - 1]
    ACC2 = [FULL, *range(G1, FULL)]
    U_ORDER = [*range(G1), *ACC2]

    def rows(t):
        return TAIL if t == NT - 1 else P

    def bank2(m):
        return (7, 0, 1, 2, 6)[m - G1]

    early_tiles = [m for m in ACC2 if bank2(m) in TRB]
    BANK3 = (3, 4)
    LAST3 = (5, 6)

    chunks = []
    chunks_after = []
    rowchunks_after = []
    for k in range(NT):
        cuts = sorted({*range(k, NT, TR)} if k else {*range(0, G1, TR), *range(G1, NT, TR)}) + [NT]
        for i0, i1 in zip(cuts, cuts[1:]):
            chunks.append(("row", k, i0, i1))
        rowchunks_after.append(len(chunks))
        for i in range(k + 1, NT, TR):
            chunks.append(("col", k, i, min(i + TR, NT)))
        chunks_after.append(len(chunks))

    def step_chunks(k):
        return range(chunks_after[k - 1] if k else 0, chunks_after[k])

    N1, N2 = NT, 2 * NT
    NN = N2 + 2 * NT

    HALVES = ((0, G1), (G1, NT))
    X_USES = [len(range(s, NT, NX)) for s in range(NX)]

    def at_split(i, h):
        return i * 2 + (N2 + h)

    def at_slot(e, h):
        return (N2 + 2 * e + h) % NSPLIT

    ctx = ExitStack()
    with ctx:
        def sb(name, shape, dt=fp32):
            return ctx.enter_context(nc.sbuf_tensor(name, shape, dt))

        def sem(name):
            return ctx.enter_context(nc.semaphore(name))

        A = sb("A", [P, NT, N])
        S = sb("S", [P, 2, N])
        AT = sb("AT", [P, NT, N])
        w_hi = sb("w_hi", [P, NSPLIT, SW], f32r)
        w_lo = sb("w_lo", [P, NSPLIT, SW], f32r)
        v_hi = sb("v_hi", [P, NT, D], f32r)
        v_lo = sb("v_lo", [P, NT, D], f32r)
        v_x = sb("v_x", [P, D], f32r)
        xs = sb("xs", [P, NX, D])
        ident = sb("ident", [P, P])
        ident2 = sb("ident2", [P, P])
        sums = sb("sums", [P, NT, 2])
        deg = sb("deg", [P, NT])
        positive = sb("positive", [P, NT])
        power = sb("power", [P, NT])
        dinv = sb("dinv", [P, NT])
        dinvh = sb("dinvh", [P, NT])
        mhalf = sb("mhalf", [P, 1])
        stats = sb("stats", [P, 2, 6])
        mv = sb("mv", [P, 2, 2])
        veps = sb("veps", [P, 2])
        rstd = sb("rstd", [P, 2])
        bank = [ctx.enter_context(nc.psum_tensor(f"bank{b}", [P, 512], fp32)) for b in range(NBANK)]

        strip_here = [sem(f"strip_here{k}") for k in range(NT)]
        first_here = [sem(f"first_here{j}") for j in range(4)]
        tail_here = sem("tail_here")
        warm_done = sem("warm_done")
        kept = sem("kept")
        deg_done = sem("deg_done")
        x_here = [sem(f"x_here{s}") for s in range(NX)]
        fills = sem("fills")
        consts = sem("consts")
        tr_done = sem("tr_done")
        tr_out = sem("tr_out")
        diag_done = sem("diag_done")
        s_done = sem("s_done")
        mask_done = sem("mask_done")
        pow_done = sem("pow_done")
        dinv_done = sem("dinv_done")
        hi_done = sem("hi_done")
        lo_done = sem("lo_done")
        z_hi = sem("z_hi")
        z_lo = sem("z_lo")
        mm_done = sem("mm_done")
        acc_done = sem("acc_done")
        dinvh_done = sem("dinvh_done")
        u_raw = sem("u_raw")
        u_hi = sem("u_hi")
        u_lo = sem("u_lo")
        z_packed = sem("z_packed")
        u_packed = sem("u_packed")
        s1_packed = sem("s1_packed")
        s_packed = sem("s_packed")
        at_packed = [sem(f"at_packed{j}") for j in range(2)]
        res_done = sem("res_done")
        half_done = sem("half_done")
        stats_done = sem("stats_done")
        mean_done = sem("mean_done")
        veps_done = sem("veps_done")
        rstd_done = sem("rstd_done")
        ln_done = sem("ln_done")
        out_done = [sem(f"out_done{e}") for e in range(2)]

        block = ctx.enter_context(nc.Block())

        def wait_acc(eng, m):
            if m == G1 - 1:
                eng.wait_ge(mm_done, N1)
            elif m == ACC2[-1]:
                eng.wait_ge(mm_done, N2)
            else:
                eng.wait_ge(acc_done, m + 1 if m < G1 else G1 + ACC2.index(m))

        @block.sync
        def _(sp):
            def load_x(k):
                if k >= NX:
                    sp.wait_ge(z_hi, k - NX + 1)
                    sp.wait_ge(z_lo, k - NX + 1)
                sp.dma_start(xs[:rows(k), k % NX, :], x[k * P:k * P + rows(k), :]).then_inc(x_here[k % NX], 16)

            def load_residual(i, e, p):
                sp.dma_start(xs[:p, e, :], x[bass.ds(i * P, p), :]).then_inc(x_here[e], 16)

            def blocks(t0, t1):
                return A[:, t0:t1, 0:P], adj[t0 * P:t1 * P, 0:P].rearrange("(t p) c -> p t c", p=P)

            sp.dma_start(*blocks(0, TR)).then_inc(first_here[0], 16)
            sp.dma_start(*blocks(TR, G1)).then_inc(first_here[1], 16)
            sp.dma_start(A[:, 0, P:SW], adj[0:P, P:SW]).then_inc(first_here[1], 16)
            sp.dma_start(*blocks(G1, FULL)).then_inc(first_here[2], 16)
            sp.dma_start(A[0:64, FULL, 0:P], adj[FULL * P:FULL * P + 64, 0:P]).then_inc(first_here[3], 16)
            sp.dma_start(A[64:TAIL, FULL, 0:P], adj[FULL * P + 64:N, 0:P]).then_inc(first_here[3], 16)
            sp.dma_start(A[:, 0, SW:N], adj[0:P, SW:N]).then_inc(first_here[3], 16)
            load_x(0)
            for k in range(1, NT):
                r, c = k * P, (k + 1) * P
                if k == 1:
                    sp.dma_start(A[0:64, FULL, P:N], adj[FULL * P:FULL * P + 64, P:N]).then_inc(tail_here, 16)
                    sp.dma_start(A[64:TAIL, FULL, P:N], adj[FULL * P + 64:N, P:N]).then_inc(tail_here, 16)
                if k < FULL:
                    sp.dma_start(A[:, k, r:N], adj[r:c, r:N]).then_inc(strip_here[k], 16)
                if k + 1 < FULL:
                    sp.dma_start(A[:, k + 1:FULL, r:c],
                                 adj[c:FULL * P, r:c].rearrange("(t p) c -> p t c", p=P)).then_inc(strip_here[k], 16)
                load_x(k)
            for e in range(2):
                k = (X_USES[e] - 1) * NX + e
                sp.wait_ge(z_hi, k + 1)
                sp.wait_ge(z_lo, k + 1)
                load_residual(e, e, P)

            def words(ap):
                return ap.bitcast(fp32)

            def pack_v_high(done):
                sp.dma_start(words(v_x[0:64, :]), words(v_hi[0:64, FULL, :])).then_inc(done, 16)
                sp.dma_start(words(v_x[64:TAIL, :]), words(v_hi[64:TAIL, FULL, :])).then_inc(done, 16)

            def pack_v_low(done):
                sp.dma_start(words(v_hi[TAIL:TAIL + DUP1, FULL, :]), words(v_lo[0:DUP1, FULL, :])).then_inc(done, 16)
                sp.dma_start(words(v_x[TAIL:TAIL + DUP2, :]), words(v_lo[DUP1:TAIL, FULL, :])).then_inc(done, 16)

            def pack_w(n, s, c0, c1, done):
                sp.wait_ge(hi_done, n + 1)
                sp.wait_ge(lo_done, n + 1)
                high, low = w_hi[:, s, c0:c1], w_lo[:, s, c0:c1]
                sp.dma_start(words(high[TAIL:TAIL + DUP1, :]), words(high[0:DUP1, :])).then_inc(done, 16)
                sp.dma_start(words(low[TAIL:TAIL + DUP2, :]), words(high[DUP1:TAIL, :])).then_inc(done, 16)

            def pack_at(i, e, m):
                c = (FULL - G1) * m
                pack_w(at_split(i, 1), at_slot(e, 1), c, c + m, at_packed[e])

            def store(i, e, p):
                sp.wait_ge(ln_done, i + 1)
                sp.dma_start(out[bass.ds(i * P, p), :], xs[:p, e, :]).then_inc(out_done[e], 16)

            def refill(i, e, p):
                sp.wait_ge(out_done[e], i * 8 - 8 * e)
                load_residual(i, e, p)

            pack_w(FULL, FULL % NSPLIT, 0, SW, s1_packed)
            sp.wait_ge(z_hi, NT)
            pack_v_high(z_packed)
            sp.wait_ge(z_lo, NT)
            pack_v_low(z_packed)
            n = N1 + PASS2.index(FULL)
            pack_w(n, n % NSPLIT, 0, N - SW, s_packed)
            sp.wait_ge(mm_done, N2 - 1)
            sp.wait_ge(u_lo, G1 + 1)
            pack_v_high(u_packed)
            pack_v_low(u_packed)
            pack_at(0, 0, P)
            with sp.Fori(0, FULL - 3, 2) as i:
                for e in range(2):
                    pack_at(i + (e + 1), 1 - e, P)
                    store(i + e, e, P)
                    refill(i + (e + 2), e, P)
            pack_at(FULL - 1, 1, P)
            pack_at(FULL, 0, TAIL)
            store(FULL - 2, 0, P)
            refill(FULL, 0, TAIL)
            store(FULL - 1, 1, P)
            store(FULL, 0, TAIL)
            sp.wait_ge(out_done[0], 16 * ((NT + 1) // 2))
            sp.wait_ge(out_done[1], 16 * (NT // 2))

        @block.gpsimd
        def _(pool):
            nc.gpsimd.memset(ident[:], 0.0).then_inc(fills, 1)
            nc.gpsimd.memset(ident2[:], 0.0).then_inc(fills, 1)
            pool.wait_ge(fills, 2)
            nc.gpsimd.affine_select(out=ident[:], in_=ident[:], compare_op=ALU.not_equal, fill=1.0, base=0,
                                    pattern=[[-1, P]], channel_multiplier=1).then_inc(consts, 1)
            nc.gpsimd.affine_select(out=ident2[:], in_=ident2[:], compare_op=ALU.not_equal, fill=2.0, base=0,
                                    pattern=[[-1, P]], channel_multiplier=1).then_inc(consts, 1)
            nc.gpsimd.memset(mhalf[:], -0.5).then_inc(consts, 1)
            pool.wait_ge(consts, 3)
            nc.gpsimd.memset(AT[64:P, FULL, :], 0.0).then_inc(consts, 1)
            pool.wait_ge(consts, 4)
            for k in range(NT):
                p, r = rows(k), k * P
                pool.wait_ge(tr_done, (chunks_after[k - 1] if k else 0) + 1)
                nc.gpsimd.tensor_tensor(A[:p, k, r:r + p], A[:p, k, r:r + p], ident2[:p, :p],
                                        ALU.add).then_inc(diag_done, 1)
                pool.wait_ge(deg_done, k + 1)
                nc.gpsimd.tensor_tensor(power[:p, k:k + 1], deg[:p, k:k + 1], mhalf[:p, :],
                                        ALU.pow).then_inc(pow_done, 1)

            def root(i, e, p):
                pool.wait_ge(veps_done, i + 1)
                nc.gpsimd.tensor_tensor(rstd[:p, e:e + 1], veps[:p, e:e + 1], mhalf[:p, :],
                                        ALU.pow).then_inc(rstd_done, 1)

            with pool.Fori(0, FULL - 1, 2) as i:
                for e in range(2):
                    root(i + e, e, P)
            root(FULL, 0, TAIL)

        def split_source(n):
            if n < N1:
                return S[:rows(n), n % 2, 0:SW], rows(n), SW
            k = PASS2[n - N1]
            return A[:rows(k), k, SW:N], rows(k), N - SW

        def slot(w, n):
            src, p, width = split_source(n)
            return w[:p, n % NSPLIT, 0:width]

        def at_source(i, h, m):
            k0, k1 = HALVES[h]
            return AT[:, k0:k1, bass.ds(i * P, m)]

        def at_part(w, e, h, m):
            k0, k1 = HALVES[h]
            return w[:, at_slot(e, h), 0:(k1 - k0) * m].rearrange("p (k c) -> p k c", c=m)

        @block.scalar
        def _(act):
            def hi(n):
                if n < N1:
                    act.wait_ge(s_done, 2 * n + 1)
                else:
                    act.wait_ge(kept, PASS2[n - N1] + 1)
                if n >= NSPLIT:
                    act.wait_ge(mm_done, n - NSPLIT + 1)
                nc.scalar.activation(slot(w_hi, n), split_source(n)[0], ACT.Copy).then_inc(hi_done, 1)

            def at_hi(i, e, h, m):
                act.wait_ge(mm_done, at_split(i, h) - (NSPLIT - 1))
                nc.scalar.activation(at_part(w_hi, e, h, m), at_source(i, h, m), ACT.Copy).then_inc(hi_done, 1)

            def u_high(m):
                act.wait_ge(mm_done, N1 + PASS2.index(m) + 1)
                if m < G1:
                    act.wait_ge(u_raw, m + 1)
                    nc.scalar.activation(v_hi[:, m, :], A[:, m, 0:D], ACT.Copy).then_inc(u_hi, 1)
                else:
                    p = rows(m)
                    wait_acc(act, m)
                    nc.scalar.activation(v_hi[:p, m, :], bank[bank2(m)][:p, :], ACT.Copy,
                                         scale=dinvh[:p, m:m + 1]).then_inc(u_hi, 1)

            def evacuate(c):
                kind, k, i0, i1 = chunks[c]
                act.wait_ge(tr_done, c + 1)
                src = bank[TRB[c % 2]]
                if kind == "row":
                    w = min(i1 * P, N) - i0 * P
                    nc.scalar.activation(AT[:rows(k), k, i0 * P:i0 * P + w], src[:rows(k), 0:w],
                                         ACT.Copy).then_inc(tr_out, 1)
                    return
                full = min(i1, FULL)
                if full > i0:
                    ins = nc.scalar.activation(AT[:, i0:full, k * P:(k + 1) * P],
                                               src[:, 0:(full - i0) * P].rearrange("p (t c) -> p t c", c=P),
                                               ACT.Copy)
                if i1 == NT:
                    ins = nc.scalar.activation(AT[:TAIL, FULL, k * P:(k + 1) * P],
                                               src[:TAIL, (FULL - i0) * P:(NT - i0) * P], ACT.Copy)
                ins.then_inc(tr_out, 1)

            def keep(k):
                act.wait_ge(s_done, 2 * k + 2)
                nc.scalar.activation(A[:rows(k), k, SW:N], S[:rows(k), k % 2, SW:N], ACT.Copy).then_inc(kept, 1)

            act.wait_ge(consts, 4)
            nc.scalar.activation(AT[:, 0, 0:1], ident[:, 0:1], ACT.Copy).then_inc(warm_done, 1)
            act.wait_ge(warm_done, 1)
            for k in range(NT):
                cols = range(rowchunks_after[k], chunks_after[k])
                if k <= S_AHEAD:
                    for c in range(chunks_after[k - 1] if k else 0, rowchunks_after[k]):
                        evacuate(c)
                    if k:
                        keep(k - 1)
                for c in cols[:1 if k else 0]:
                    evacuate(c)
                hi(k)
                for c in cols[1 if k else 0:]:
                    evacuate(c)
                if S_AHEAD <= k < NT - 1:
                    for c in range(chunks_after[k], rowchunks_after[k + 1]):
                        evacuate(c)
                p = rows(k)
                act.wait_ge(dinv_done, k + 1)
                act.wait_ge(x_here[k % NX], 16 * (k // NX + 1))
                nc.scalar.activation(v_hi[:p, k, :], xs[:p, k % NX, :], ACT.Copy,
                                     scale=dinv[:p, k:k + 1]).then_inc(z_hi, 1)
                if k >= S_AHEAD:
                    keep(k)
            for n in range(N1, N1 + 3):
                hi(n)
            act.wait_ge(dinvh_done, NT)
            for m in range(G1):
                wait_acc(act, m)
                nc.scalar.activation(A[:, m, 0:D], bank[m][:, :], ACT.Copy,
                                     scale=dinvh[:, m:m + 1]).then_inc(u_raw, 1)
            hi(N1 + 3)
            for n in range(N1 + 4, N2):
                hi(n)
                if n - N1 - 4 < G1:
                    u_high(n - N1 - 4)
            at_hi(0, 0, 0, P)
            at_hi(0, 0, 1, P)
            at_hi(1, 1, 0, P)
            for m in ACC2:
                u_high(m)
            at_hi(1, 1, 1, P)
            with act.Fori(2, FULL - 1, 2) as i:
                for e in range(2):
                    at_hi(i + e, e, 0, P)
                    at_hi(i + e, e, 1, P)
            at_hi(FULL, 0, 0, TAIL)
            at_hi(FULL, 0, 1, TAIL)

        @block.vector
        def _(dve):
            def lo(n):
                dve.wait_ge(hi_done, n + 1)
                if n >= NSPLIT:
                    dve.wait_ge(mm_done, n - NSPLIT + 1)
                nc.vector.tensor_tensor(slot(w_lo, n), split_source(n)[0], slot(w_hi, n).bitcast(fp32),
                                        ALU.subtract).then_inc(lo_done, 1)

            def at_lo(i, e, h, m):
                dve.wait_ge(hi_done, at_split(i, h) + 1)
                dve.wait_ge(mm_done, at_split(i, h) - (NSPLIT - 1))
                nc.vector.tensor_tensor(at_part(w_lo, e, h, m), at_source(i, h, m),
                                        at_part(w_hi, e, h, m).bitcast(fp32), ALU.subtract).then_inc(lo_done, 1)

            def u_low(m):
                p = rows(m)
                dve.wait_ge(u_hi, U_ORDER.index(m) + 1)
                if m < G1:
                    nc.vector.tensor_tensor(v_lo[:, m, :], A[:, m, 0:D], v_hi[:, m, :].bitcast(fp32),
                                            ALU.subtract).then_inc(u_lo, 1)
                else:
                    nc.vector.scalar_tensor_tensor(v_lo[:p, m, :], bank[bank2(m)][:p, :], dinvh[:p, m:m + 1],
                                                   v_hi[:p, m, :].bitcast(fp32), ALU.mult,
                                                   ALU.subtract).then_inc(u_lo, 1)

            def add_residual(i, e, p, b, h=0, c0=0, c1=D):
                nc.vector.tensor_tensor(xs[:p, e, c0:c1], bank[b][:p, c0:c1], xs[:p, e, c0:c1],
                                        ALU.add).then_inc(res_done, 1)
                dve.wait_ge(res_done, i + (h + 1))
                nc.vector.bn_stats(stats[:p, (e + h) % 2, :], xs[:p, e, c0:c1]).then_inc(stats_done, 1)

            def normalise(i, e, p, st):
                nc.vector.bn_aggr(mv[:p, e, :], st).then_inc(mean_done, 1)
                dve.wait_ge(mean_done, i + 1)
                nc.vector.tensor_scalar(veps[:p, e:e + 1], mv[:p, e, 1:2], EPS, None, ALU.add).then_inc(veps_done, 1)
                dve.wait_ge(rstd_done, i + 1)
                nc.vector.tensor_scalar(xs[:p, e, :], xs[:p, e, :], mv[:p, e, 0:1], rstd[:p, e:e + 1],
                                        ALU.subtract, ALU.mult).then_inc(ln_done, 1)

            def residual(i, e):
                dve.wait_ge(x_here[e], i * 8 + (16 * (X_USES[e] + 1) - 8 * e))
                dve.wait_ge(mm_done, at_split(i, 1) + 1)
                add_residual(i, e, P, BANK3[e])
                dve.wait_ge(stats_done, i + 1)

            def finish_last():
                dve.wait_ge(x_here[0], 16 * (X_USES[0] + FULL // 2 + 1))
                for h in range(2):
                    dve.wait_ge(half_done, h + 1)
                    add_residual(FULL, 0, TAIL, LAST3[h], h, h * D // 2, (h + 1) * D // 2)
                dve.wait_ge(stats_done, FULL + 2)
                normalise(FULL, 0, TAIL, stats[:TAIL, :, :])

            def form_s(k):
                p = rows(k)
                if k >= 2:
                    dve.wait_ge(kept, k - 1)
                for h, (c0, c1) in enumerate(((0, SW), (SW, N))):
                    if k == 0:
                        dve.wait_ge(tr_out, 2 if h == 0 else rowchunks_after[0])
                    else:
                        dve.wait_ge(tr_out, rowchunks_after[k])
                    dve.wait_ge(diag_done, k + 1)
                    if k == 0:
                        dve.wait_ge(first_here[1 + 2 * h], 32 + 16 * h)
                    nc.vector.scalar_tensor_tensor(S[:p, k % 2, c0:c1], A[:p, k, c0:c1], 1.0, AT[:p, k, c0:c1],
                                                   ALU.mult, ALU.add,
                                                   accum_out=sums[:p, k, h:h + 1]).then_inc(s_done, 1)

            for k in range(NT):
                p = rows(k)
                if k <= S_AHEAD:
                    form_s(k)
                dve.wait_ge(s_done, 2 * k + 2)
                nc.vector.tensor_scalar(deg[:p, k:k + 1], sums[:p, k, 0:1], sums[:p, k, 1:2], 0.5, ALU.add,
                                        ALU.mult).then_inc(deg_done, 1)
                dve.wait_ge(deg_done, k + 1)
                nc.vector.tensor_scalar(positive[:p, k:k + 1], deg[:p, k:k + 1], 0.0, None,
                                        ALU.is_gt).then_inc(mask_done, 1)
                if k >= 2:
                    lo(k)
                dve.wait_ge(pow_done, k + 1)
                dve.wait_ge(mask_done, k + 1)
                nc.vector.tensor_scalar(dinv[:p, k:k + 1], power[:p, k:k + 1], BIG, positive[:p, k:k + 1],
                                        ALU.min, ALU.mult).then_inc(dinv_done, 1)
                if k < 2:
                    lo(k)
                if S_AHEAD <= k < NT - 1:
                    form_s(k + 1)
                dve.wait_ge(z_hi, k + 1)
                nc.vector.scalar_tensor_tensor(v_lo[:p, k, :], xs[:p, k % NX, :], dinv[:p, k:k + 1],
                                               v_hi[:p, k, :].bitcast(fp32), ALU.mult, ALU.subtract).then_inc(z_lo, 1)
                nc.vector.tensor_scalar(dinvh[:p, k:k + 1], dinv[:p, k:k + 1], 0.5, None,
                                        ALU.mult).then_inc(dinvh_done, 1)
            dve.wait_ge(dinvh_done, NT)
            for n in range(N1, N1 + 4):
                lo(n)
            for n in range(N1 + 4, N2):
                lo(n)
                if n - N1 - 4 < G1:
                    u_low(n - N1 - 4)
            at_lo(0, 0, 0, P)
            at_lo(0, 0, 1, P)
            at_lo(1, 1, 0, P)
            for m in ACC2:
                u_low(m)
            at_lo(1, 1, 1, P)
            with dve.Fori(2, FULL - 1, 2) as i:
                for e in range(2):
                    at_lo(i + e, e, 0, P)
                    residual(i + (e - 2), e)
                    at_lo(i + e, e, 1, P)
                    normalise(i + (e - 2), e, P, stats[:, e, :])
            at_lo(FULL, 0, 0, TAIL)
            residual(FULL - 2, 0)
            at_lo(FULL, 0, 1, TAIL)
            normalise(FULL - 2, 0, P, stats[:, 0, :])
            residual(FULL - 1, 1)
            normalise(FULL - 1, 1, P, stats[:, 1, :])
            finish_last()

        @block.tensor
        def _(pe):
            def transposes(c):
                kind, k, i0, i1 = chunks[c]
                if c >= 2:
                    pe.wait_ge(tr_out, c - 1)
                dst = bank[TRB[c % 2]]
                for i in range(i0, i1):
                    at = (i - i0) * P
                    if kind == "row":
                        src, p, w = A[:rows(i), i, k * P:k * P + rows(k)], rows(k), rows(i)
                    else:
                        src, p, w = A[:rows(k), k, i * P:i * P + rows(i)], rows(i), rows(k)
                    last = nc.tensor.transpose(dst[:p, at:at + w], src, ident[:w, :w])
                last.then_inc(tr_done, 1)

            def product(s, dst, col, k, first, last, step=0, c0=0, c1=D):
                p, m = rows(k), dst.shape[0]
                hi, lo = w_hi[:p, s, col:col + m], w_lo[:p, s, col:col + m]
                if step:
                    pe.wait_ge(hi_done, step)
                    pe.wait_ge(z_hi, step)
                nc.tensor.matmul(dst, hi, v_hi[:p, k, c0:c1], start=first, stop=False)
                if step:
                    pe.wait_ge(lo_done, step)
                nc.tensor.matmul(dst, lo, v_hi[:p, k, c0:c1], start=False, stop=False)
                if step:
                    pe.wait_ge(z_lo, step)
                return nc.tensor.matmul(dst, hi, v_lo[:p, k, c0:c1], start=False, stop=last)

            def packed_product(s, dst, col, first, last, c0=0, c1=D):
                p1, p2, m = TAIL + DUP1, TAIL + DUP2, dst.shape[0]
                nc.tensor.matmul(dst, w_hi[:p1, s, col:col + m], v_hi[:p1, FULL, c0:c1], start=first, stop=False)
                return nc.tensor.matmul(dst, w_lo[:p2, s, col:col + m], v_x[:p2, c0:c1], start=False, stop=last)

            def next_transposes():
                c = pending.pop(0)
                k = chunks[c][1]
                if c == chunks_after[k - 1]:
                    if k < FULL:
                        pe.wait_ge(strip_here[k], 32 if k + 1 < FULL else 16)
                    if k == 1:
                        pe.wait_ge(tail_here, 32)
                transposes(c)

            def warm_up(n):
                for _ in range(n):
                    nc.tensor.matmul(bank[0][:, 0:P], ident[:, :], ident[:, :], start=True, stop=True)

            pe.wait_ge(consts, 1)
            warm_up(WARM)
            for c in step_chunks(0):
                if c == 0:
                    pe.wait_ge(first_here[0], 16)
                elif c == 1:
                    pe.wait_ge(first_here[1], 32)
                elif c == 2:
                    pe.wait_ge(first_here[2], 16)
                elif c == 3:
                    pe.wait_ge(first_here[3], 48)
                transposes(c)
            pending = list(range(chunks_after[0], len(chunks)))
            warm_up(WARM2)
            for k in range(FULL):
                if k == 1:
                    next_transposes()
                    next_transposes()
                for m in range(G1):
                    for _ in range((0, 2, 1, 1, 1, 1)[m] if k == 0 else 1):
                        if pending and chunks[pending[0]][1] <= k + (AHEAD if k else 1):
                            next_transposes()
                    ins = product(k % NSPLIT, bank[m][:, :], m * P, k, k == 0, False, k + 1 if m == 0 else 0)
                ins.then_inc(mm_done, 1)
            pe.wait_ge(tr_out, len(chunks))
            for n in range(N1, N1 + EARLY):
                pe.wait_ge(hi_done, n + 1)
                pe.wait_ge(lo_done, n + 1)
                for m in early_tiles:
                    product(n % NSPLIT, bank[bank2(m)][:rows(m), :], (m - G1) * P, PASS2[n - N1], n == N1, False)
            pe.wait_ge(z_packed, 64)
            pe.wait_ge(s1_packed, 32)
            for m in range(G1):
                ins = packed_product(FULL % NSPLIT, bank[m][:, :], m * P, False, True)
                if m < G1 - 1:
                    ins.then_inc(acc_done, 1)
                else:
                    ins.then_inc(mm_done, 1)
            for n in range(N1, N2):
                k = PASS2[n - N1]
                pe.wait_ge(hi_done, n + 1)
                pe.wait_ge(lo_done, n + 1)
                if k == FULL:
                    pe.wait_ge(s_packed, 32)
                for m in ACC2:
                    if n < N1 + EARLY and m in early_tiles:
                        continue
                    if n == N1:
                        pe.wait_ge(u_raw, bank2(m) + 1)
                    dst, col = bank[bank2(m)][:rows(m), :], (m - G1) * P
                    if k == FULL:
                        ins = packed_product(n % NSPLIT, dst, col, False, False)
                    else:
                        ins = product(n % NSPLIT, dst, col, k, n == N1, n == N2 - 1)
                    if n == N2 - 1 and m != ACC2[-1]:
                        ins.then_inc(acc_done, 1)
                ins.then_inc(mm_done, 1)

            def at_products(i, e):
                for h, (k0, k1) in enumerate(HALVES):
                    pe.wait_ge(hi_done, at_split(i, h) + 1)
                    pe.wait_ge(lo_done, at_split(i, h) + 1)
                    if h == 0 and isinstance(i, int):
                        pe.wait_ge(u_raw, BANK3[e] + 1)
                    elif h == 0:
                        pe.wait_ge(res_done, i - 1)
                    for k in range(k0, min(k1, FULL)):
                        if isinstance(i, int) and i == 0:
                            pe.wait_ge(u_lo, U_ORDER.index(k) + 1)
                        ins = product(at_slot(e, h), bank[BANK3[e]][:, :], (k - k0) * P, k, k == 0, False)
                    if k1 == NT:
                        if isinstance(i, int) and i == 0:
                            pe.wait_ge(u_packed, 64)
                        pe.wait_ge(at_packed[e], i * 16 + (32 - 16 * e))
                        ins = packed_product(at_slot(e, h), bank[BANK3[e]][:, :], (FULL - k0) * P, False, True)
                    ins.then_inc(mm_done, 1)

            at_products(0, 0)
            at_products(1, 1)
            with pe.Fori(2, FULL - 1, 2) as i:
                for e in range(2):
                    at_products(i + e, e)
            pe.wait_ge(hi_done, NN)
            pe.wait_ge(lo_done, NN)
            pe.wait_ge(at_packed[0], 16 * FULL + 32)
            for g in range(2):
                if g == 0:
                    pe.wait_ge(u_raw, G1)
                else:
                    pe.wait_ge(u_lo, NT)
                c0, c1 = g * D // 2, (g + 1) * D // 2
                dst = bank[LAST3[g]][:TAIL, c0:c1]
                for h, (k0, k1) in enumerate(HALVES):
                    for k in range(k0, min(k1, FULL)):
                        product(at_slot(0, h), dst, (k - k0) * TAIL, k, k == 0, False, 0, c0, c1)
                ins = packed_product(at_slot(0, 1), dst, (FULL - G1) * TAIL, False, True, c0, c1)
                ins.then_inc(half_done, 1)


_INS = ["x", "adj"]


def kernel(**inputs):
    import numpy as _np
    import concourse.bacc as _bacc
    from concourse import mybir as _mybir
    from concourse.bass_utils import run_bass_kernel_spmd as _run

    nc = _bacc.Bacc("TRN2", target_bir_lowering=False, num_devices=1)
    arrays, args = {}, []
    for name in _INS:
        a = _np.ascontiguousarray(inputs[name])
        arrays[f"in_{name}"] = a
        args.append(nc.dram_tensor(f"in_{name}", a.shape, _mybir.dt.from_np(a.dtype), kind="ExternalInput").ap())
    shape = inputs["x"].shape
    args.append(nc.dram_tensor("out", shape, _mybir.dt.from_np(_np.dtype("float32")), kind="ExternalOutput").ap())
    gcn_residual_layernorm_kernel(nc, *args)
    r = _run(nc, [arrays], core_ids=[0])
    return r.results[0]["out"]
```
